# Optimizing a Trainium2 kernel written in Bass

```python
import numpy as np
import jax
import jax.numpy as jnp

def _softmax(x, axis=-1):
    return jax.nn.softmax(x, axis=axis)

def _gelu(x):
    return jax.nn.gelu(x, approximate=True)

def _silu(x):
    return jax.nn.silu(x)

def _sigmoid(x):
    return jax.nn.sigmoid(x)

def _layernorm(x, axis=-1, eps=1e-05):
    m = jnp.mean(x, axis=axis, keepdims=True)
    v = jnp.var(x, axis=axis, keepdims=True)
    return (x - m) / jnp.sqrt(v + eps)

def _scatter_add(tgt, idx, src, axis=0):
    return tgt.at[idx].add(src)

def _segment_sum(src, seg, n):
    return jax.ops.segment_sum(src, seg, n)
kernel_name = 'mk_dlrm_tower_d1_rec_r8_9b7a50'

def setup_inputs(seed: int=0):
    np.random.seed(seed)
    _w = jnp.asarray

    def _rec_inputs():
        import jax
        import jax.numpy as jnp
        _tk = jax.random.key(seed)
        ids = jnp.stack([jax.random.randint(jax.random.fold_in(_tk, 200 + f), (2048,), 0, v, jnp.int32) for f, v in enumerate([1250, 1250, 125000, 1250, 1000, 1250, 12500, 1000, 1250, 1000, 1250, 1000, 1000, 1250, 1250, 1000, 1250, 12500, 12500, 12500, 1000, 1250, 12500, 1250, 1000, 12500, 12500])], axis=1)
        tbl_0 = 0.05 * jax.random.normal(jax.random.fold_in(_tk, 500 + 0), (1250, 128), jnp.float32)
        tbl_1 = 0.05 * jax.random.normal(jax.random.fold_in(_tk, 500 + 1), (1250, 128), jnp.float32)
        tbl_2 = 0.05 * jax.random.normal(jax.random.fold_in(_tk, 500 + 2), (125000, 128), jnp.float32)
        tbl_3 = 0.05 * jax.random.normal(jax.random.fold_in(_tk, 500 + 3), (1250, 128), jnp.float32)
        tbl_4 = 0.05 * jax.random.normal(jax.random.fold_in(_tk, 500 + 4), (1000, 128), jnp.float32)
        tbl_5 = 0.05 * jax.random.normal(jax.random.fold_in(_tk, 500 + 5), (1250, 128), jnp.float32)
        tbl_6 = 0.05 * jax.random.normal(jax.random.fold_in(_tk, 500 + 6), (12500, 128), jnp.float32)
        tbl_7 = 0.05 * jax.random.normal(jax.random.fold_in(_tk, 500 + 7), (1000, 128), jnp.float32)
        tbl_8 = 0.05 * jax.random.normal(jax.random.fold_in(_tk, 500 + 8), (1250, 128), jnp.float32)
        tbl_9 = 0.05 * jax.random.normal(jax.random.fold_in(_tk, 500 + 9), (1000, 128), jnp.float32)
        tbl_10 = 0.05 * jax.random.normal(jax.random.fold_in(_tk, 500 + 10), (1250, 128), jnp.float32)
        tbl_11 = 0.05 * jax.random.normal(jax.random.fold_in(_tk, 500 + 11), (1000, 128), jnp.float32)
        tbl_12 = 0.05 * jax.random.normal(jax.random.fold_in(_tk, 500 + 12), (1000, 128), jnp.float32)
        tbl_13 = 0.05 * jax.random.normal(jax.random.fold_in(_tk, 500 + 13), (1250, 128), jnp.float32)
        tbl_14 = 0.05 * jax.random.normal(jax.random.fold_in(_tk, 500 + 14), (1250, 128), jnp.float32)
        tbl_15 = 0.05 * jax.random.normal(jax.random.fold_in(_tk, 500 + 15), (1000, 128), jnp.float32)
        tbl_16 = 0.05 * jax.random.normal(jax.random.fold_in(_tk, 500 + 16), (1250, 128), jnp.float32)
        tbl_17 = 0.05 * jax.random.normal(jax.random.fold_in(_tk, 500 + 17), (12500, 128), jnp.float32)
        tbl_18 = 0.05 * jax.random.normal(jax.random.fold_in(_tk, 500 + 18), (12500, 128), jnp.float32)
        tbl_19 = 0.05 * jax.random.normal(jax.random.fold_in(_tk, 500 + 19), (12500, 128), jnp.float32)
        tbl_20 = 0.05 * jax.random.normal(jax.random.fold_in(_tk, 500 + 20), (1000, 128), jnp.float32)
        tbl_21 = 0.05 * jax.random.normal(jax.random.fold_in(_tk, 500 + 21), (1250, 128), jnp.float32)
        tbl_22 = 0.05 * jax.random.normal(jax.random.fold_in(_tk, 500 + 22), (12500, 128), jnp.float32)
        tbl_23 = 0.05 * jax.random.normal(jax.random.fold_in(_tk, 500 + 23), (1250, 128), jnp.float32)
        tbl_24 = 0.05 * jax.random.normal(jax.random.fold_in(_tk, 500 + 24), (1000, 128), jnp.float32)
        tbl_25 = 0.05 * jax.random.normal(jax.random.fold_in(_tk, 500 + 25), (12500, 128), jnp.float32)
        tbl_26 = 0.05 * jax.random.normal(jax.random.fold_in(_tk, 500 + 26), (12500, 128), jnp.float32)
        _rk = jax.random.fold_in(_tk, 7)
        r_bottom_mlp_out = 4.13588e-05 + 0.999923 * jax.random.normal(jax.random.fold_in(_rk, 101), (2048, 128), jnp.float32)
        W_top1 = 0.0405887 * jax.random.normal(jax.random.fold_in(_tk, 801), (607, 512), jnp.float32)
        W_top2 = 0.0441942 * jax.random.normal(jax.random.fold_in(_tk, 802), (512, 256), jnp.float32)
        W_top3 = 0.0625 * jax.random.normal(jax.random.fold_in(_tk, 803), (256, 1), jnp.float32)
        b_top1 = jnp.zeros((512,), jnp.float32)
        b_top2 = jnp.zeros((256,), jnp.float32)
        return (r_bottom_mlp_out, ids, tbl_0, tbl_1, tbl_2, tbl_3, tbl_4, tbl_5, tbl_6, tbl_7, tbl_8, tbl_9, tbl_10, tbl_11, tbl_12, tbl_13, tbl_14, tbl_15, tbl_16, tbl_17, tbl_18, tbl_19, tbl_20, tbl_21, tbl_22, tbl_23, tbl_24, tbl_25, tbl_26, W_top1, b_top1, W_top2, b_top2, W_top3)
    r_bottom_mlp_out, ids, tbl_0, tbl_1, tbl_2, tbl_3, tbl_4, tbl_5, tbl_6, tbl_7, tbl_8, tbl_9, tbl_10, tbl_11, tbl_12, tbl_13, tbl_14, tbl_15, tbl_16, tbl_17, tbl_18, tbl_19, tbl_20, tbl_21, tbl_22, tbl_23, tbl_24, tbl_25, tbl_26, W_top1, b_top1, W_top2, b_top2, W_top3 = _rec_inputs()

    def _L0_rec_setup():
        import jax, jax.numpy as jnp
        import numpy as np
        NUM_FEATURES = 27

        def _tril_indices(F):
            idx = []
            for i in range(F):
                for j in range(i):
                    idx.append(i * F + j)
            return np.asarray(idx, dtype=np.int32)
        TRIL_IDX = _tril_indices(NUM_FEATURES)
        key = jax.random.key(seed)
        k1, k2 = jax.random.split(key)
        B, F, D = (8192, NUM_FEATURES, 128)
        features = jax.random.normal(k1, (B, F, D), dtype=jnp.float32)
        bottom_mlp_out = jax.random.normal(k2, (B, D), dtype=jnp.float32)
        return {'features': features, 'bottom_mlp_out': bottom_mlp_out}
    _L0_rec_all = _L0_rec_setup()
    _L0_rec_in = {k: v for k, v in _L0_rec_all.items() if k in ()}
    del _L0_rec_all
    return {'r_bottom_mlp_out': r_bottom_mlp_out, 'ids': ids, 'tbl_0': tbl_0, 'tbl_1': tbl_1, 'tbl_2': tbl_2, 'tbl_3': tbl_3, 'tbl_4': tbl_4, 'tbl_5': tbl_5, 'tbl_6': tbl_6, 'tbl_7': tbl_7, 'tbl_8': tbl_8, 'tbl_9': tbl_9, 'tbl_10': tbl_10, 'tbl_11': tbl_11, 'tbl_12': tbl_12, 'tbl_13': tbl_13, 'tbl_14': tbl_14, 'tbl_15': tbl_15, 'tbl_16': tbl_16, 'tbl_17': tbl_17, 'tbl_18': tbl_18, 'tbl_19': tbl_19, 'tbl_20': tbl_20, 'tbl_21': tbl_21, 'tbl_22': tbl_22, 'tbl_23': tbl_23, 'tbl_24': tbl_24, 'tbl_25': tbl_25, 'tbl_26': tbl_26, 'W_top1': W_top1, 'b_top1': b_top1, 'W_top2': W_top2, 'b_top2': b_top2, 'W_top3': W_top3}

def reference(r_bottom_mlp_out, ids, tbl_0, tbl_1, tbl_2, tbl_3, tbl_4, tbl_5, tbl_6, tbl_7, tbl_8, tbl_9, tbl_10, tbl_11, tbl_12, tbl_13, tbl_14, tbl_15, tbl_16, tbl_17, tbl_18, tbl_19, tbl_20, tbl_21, tbl_22, tbl_23, tbl_24, tbl_25, tbl_26, W_top1, b_top1, W_top2, b_top2, W_top3):
    import jax
    import jax.numpy as jnp

    def _L0_rec_ref(features, bottom_mlp_out):
        import jax, jax.numpy as jnp
        import numpy as np
        NUM_FEATURES = 27

        def _tril_indices(F):
            idx = []
            for i in range(F):
                for j in range(i):
                    idx.append(i * F + j)
            return np.asarray(idx, dtype=np.int32)
        TRIL_IDX = _tril_indices(NUM_FEATURES)
        B = features.shape[0]
        F = features.shape[1]
        interactions = jnp.einsum('bfd,bgd->bfg', features, features)
        interactions = interactions.reshape(B, F * F)
        x = interactions[:, TRIL_IDX]
        return jnp.concatenate([bottom_mlp_out, x], axis=1)
    e = jnp.stack([tbl_0[ids[:, 0]], tbl_1[ids[:, 1]], tbl_2[ids[:, 2]], tbl_3[ids[:, 3]], tbl_4[ids[:, 4]], tbl_5[ids[:, 5]], tbl_6[ids[:, 6]], tbl_7[ids[:, 7]], tbl_8[ids[:, 8]], tbl_9[ids[:, 9]], tbl_10[ids[:, 10]], tbl_11[ids[:, 11]], tbl_12[ids[:, 12]], tbl_13[ids[:, 13]], tbl_14[ids[:, 14]], tbl_15[ids[:, 15]], tbl_16[ids[:, 16]], tbl_17[ids[:, 17]], tbl_18[ids[:, 18]], tbl_19[ids[:, 19]], tbl_20[ids[:, 20]], tbl_21[ids[:, 21]], tbl_22[ids[:, 22]], tbl_23[ids[:, 23]], tbl_24[ids[:, 24]], tbl_25[ids[:, 25]], tbl_26[ids[:, 26]]], axis=1)
    z = _L0_rec_ref(e, r_bottom_mlp_out)
    z = z.reshape(z.shape[0], -1)
    h = jnp.concatenate([z, r_bottom_mlp_out], axis=1)
    h = jnp.maximum(h @ W_top1 + b_top1, 0.0)
    h = jnp.maximum(h @ W_top2 + b_top2, 0.0)
    y = h @ W_top3
    return y

_drawn_inputs = setup_inputs


def setup_inputs(seed=0):
    import zlib

    import numpy as np

    out = dict(_drawn_inputs(seed))
    spreads = {'b_top1': (0.0, 0.1), 'b_top2': (0.0, 0.1)}
    factors = {'tbl_0': 4.819,
     'tbl_1': 5.021,
     'tbl_2': 4.639,
     'tbl_3': 4.193,
     'tbl_4': 4.854,
     'tbl_5': 4.245,
     'tbl_6': 4.813,
     'tbl_7': 4.144,
     'tbl_8': 4.621,
     'tbl_9': 4.993,
     'tbl_10': 4.418,
     'tbl_11': 4.547,
     'tbl_12': 4.575,
     'tbl_13': 4.317,
     'tbl_14': 4.791,
     'tbl_15': 4.975,
     'tbl_16': 4.67,
     'tbl_17': 4.959,
     'tbl_18': 4.199,
     'tbl_19': 4.349,
     'tbl_20': 4.445,
     'tbl_21': 4.916,
     'tbl_22': 4.785,
     'tbl_23': 4.954,
     'tbl_24': 4.453,
     'tbl_25': 5.05,
     'tbl_26': 4.662}
    for name, (base, spread) in spreads.items():
        noise = np.random.default_rng([zlib.crc32(name.encode()), seed]).standard_normal(out[name].shape)
        drawn = base * np.exp(spread * noise) if base else spread * noise
        out[name] = jnp.asarray(drawn.astype(out[name].dtype))
    for name, factor in factors.items():
        out[name] = (out[name] * factor).astype(out[name].dtype)
    return out
```

```python
from contextlib import ExitStack

import concourse.bass as bass
from concourse import mybir

F32 = mybir.dt.float32
I32 = mybir.dt.int32
U32 = mybir.dt.uint32
ALU = mybir.AluOpType
ACT = mybir.ActivationFunctionType

P = 128
QUADS = 4
QS = P // QUADS
TILES = 4
ROUND = TILES * P
BANK = 512
GROUP = BANK // P
SPAN = 8


def dlrm_tower(nc, bottom, ids, tables, w_top1, b_top1, w_top2, b_top2, w_top3, out):
    B, D = bottom.shape
    NF = len(tables)
    ROUNDS = B // ROUND
    PAIRS = NF * (NF - 1) // 2
    NG = NF - 1
    H1, H2 = w_top1.shape[1], w_top2.shape[1]
    M1, M2 = H1 // P, H2 // P
    assert D == P and w_top1.shape[0] == D + PAIRS + D and NF <= QS
    GROUPS = [list(range(a, min(a + GROUP, NF))) for a in range(0, NF, GROUP)]
    NGR = len(GROUPS)
    PAIR_ROWS = [min(P, PAIRS - a) for a in range(0, PAIRS, P)]
    CH = len(PAIR_ROWS)
    SPANS = QS // SPAN
    EXTRACTS = TILES * SPANS // 2
    PACKS = []
    for f in range(1, NF):
        k, g = f * (f - 1) // 2, 0
        while g < f:
            n = min(f - g, P - k % P)
            PACKS.append((f, g, n, k // P, k % P))
            k, g = k + n, g + n
    MLP_STEPS = 1 + M1 + M2 + 1
    assert MLP_STEPS % 2 == 0

    ids_v = ids.rearrange("(n p) f -> p n f", p=P)
    bottom_v = bottom.rearrange("(r s p) d -> r p s d", s=QUADS, p=P)
    out_v = out.rearrange("(r n) one -> r one n", n=ROUND)
    grams = nc.dram_tensor("grams", [ROUNDS, NF, NG, ROUND], F32, kind="Internal").ap()

    with ExitStack() as ctx:
        def sb(name, shape, dt=F32):
            return ctx.enter_context(nc.sbuf_tensor(name, shape, dt))

        def psum(name, shape):
            return ctx.enter_context(nc.psum_tensor(name, shape, F32))

        def sem(name):
            return ctx.enter_context(nc.semaphore(name))

        ident = sb("ident", [P, P])
        ids_all = sb("ids_all", [P, (ROUNDS + 1) * TILES, NF], I32)
        ids_now = sb("ids_now", [P, TILES, NF], I32)
        emb = sb("emb", [P, TILES, NF, D])
        embT = sb("embT", [P, 2, P, QS])
        inter = sb("inter", [P, NG, P])
        packed = sb("packed", [P, CH, ROUND])
        bot = sb("bot", [P, QUADS, D])
        botT = sb("botT", [P, ROUND])
        w1 = sb("w1", [P, CH, H1])
        w1_bot = sb("w1_bot", [P, 3, H1])
        w2 = sb("w2", [P, M1, H2])
        w3 = sb("w3", [P, M2])
        b1 = sb("b1", [P, M1])
        b2 = sb("b2", [P, M2])
        h1 = sb("h1", [P, M1, ROUND])
        h2 = sb("h2", [P, M2, ROUND])
        y = sb("y", [1, ROUND])

        tp = psum("tp", [P, 2, BANK])
        gram = psum("gram", [P, 2, SPAN, P])
        mlp = psum("mlp", [P, 2, BANK])

        weights_loaded = sem("weights_loaded")
        ids_loaded = sem("ids_loaded")
        ids_ready = sem("ids_ready")
        slots_taken = sem("slots_taken")
        ident_zeroed = sem("ident_zeroed")
        ident_ready = sem("ident_ready")
        pads_zeroed = sem("pads_zeroed")
        w1_bot_summed = sem("w1_bot_summed")
        gathered = [[sem(f"gathered_{t}_{g}") for g in range(NGR)] for t in range(TILES)]
        transposed = sem("transposed")
        evac_dve = sem("evac_dve")
        evac_act = sem("evac_act")
        grammed = sem("grammed")
        extracted_dve = sem("extracted_dve")
        extracted_act = sem("extracted_act")
        stored = sem("stored")
        packs_loaded = sem("packs_loaded")
        bot_loaded = sem("bot_loaded")
        mlp_ready = sem("mlp_ready")
        mlp_evac = sem("mlp_evac")
        y_stored = sem("y_stored")
        N_PACK_A = (len(PACKS) + 1) // 2

        block = ctx.enter_context(nc.Block())

        def rounds(eng, body):
            body(0, True)
            with eng.Fori(1, ROUNDS) as r:
                body(r, False)

        def evac_even(t, g):
            return (t * NGR + g) % 2 == 0

        def evacs_until(n):
            return (n + 1) // 2, n // 2

        @block.sync
        def _(sp):
            sp.dma_start(ids_all[:, 0:ROUNDS * TILES, :], ids_v).then_inc(ids_loaded, 16)

            def body(r, first):
                if not first:
                    sp.wait_ge(mlp_ready, r * MLP_STEPS)
                sp.dma_start(bot[:, :, :], bottom_v[r] if first else bottom_v[bass.ds(r, 1)].rearrange("o p s d -> (o p) s d")).then_inc(bot_loaded, 16)
                sp.wait_ge(extracted_dve, (r + 1) * EXTRACTS)
                sp.wait_ge(extracted_act, (r + 1) * EXTRACTS)
                dst = grams[r] if first else grams[bass.ds(r, 1)].rearrange("o f g n -> (o f) g n")
                for s in range(QUADS):
                    sp.dma_start(dst[:, :, s * P:(s + 1) * P], inter[QS * s:QS * s + NF, :, :]).then_inc(stored, 16)
                sp.wait_ge(stored, (r + 1) * 16 * QUADS)
                for f, g, n, c, k in PACKS[:N_PACK_A]:
                    sp.dma_start(packed[k:k + n, c, :], dst[f, g:g + n, :]).then_inc(packs_loaded, 16)
                sp.wait_ge(mlp_evac, (r + 1) * MLP_STEPS)
                o = out_v[r] if first else out_v[bass.ds(r, 1)].rearrange("o one n -> (o one) n")
                sp.dma_start(o, y[:, :]).then_inc(y_stored, 16)
            rounds(sp, body)
            sp.wait_ge(y_stored, 16 * ROUNDS)

        @block.gpsimd
        def _(pool):
            pool.memset(ident[:, :], 0.0).then_inc(ident_zeroed, 1)
            pool.wait_ge(ident_zeroed, 1)
            pool.affine_select(out=ident[:, :], in_=ident[:, :], compare_op=ALU.not_equal, fill=1.0,
                               base=0, pattern=[[-1, P]], channel_multiplier=1).then_inc(ident_ready, 1)
            pool.wait_ge(ids_loaded, 16)

            def body(r, first):
                for t in range(TILES):
                    if not first:
                        pool.wait_ge(ids_ready, (r - 1) * TILES + t + 1)
                        pool.wait_ge(transposed, (r - 1) * TILES * NGR + (t + 1) * NGR)
                        pool.sem_inc(slots_taken, 1)
                    idx = ids_all if first else ids_now
                    for g, features in enumerate(GROUPS):
                        for f in features:
                            pool.indirect_dma_start(
                                out=emb[:, t, f, :], out_offset=None, in_=tables[f],
                                in_offset=bass.IndirectOffsetOnAxis(ap=idx[:, t, f:f + 1].bitcast(U32), axis=0),
                            ).then_inc(gathered[t][g], 16)
            rounds(pool, body)

        @block.tensor
        def _(pe):
            pe.wait_ge(ident_ready, 1)
            pe.wait_ge(weights_loaded, 16 * (CH + 6))
            pe.wait_ge(w1_bot_summed, 1)

            def mlp_bank(r, first, n):
                if not first or n >= 2:
                    pe.wait_ge(mlp_evac, r * MLP_STEPS + n - 1)
                return mlp[:, n % 2, :]

            def body(r, first):
                pe.wait_ge(bot_loaded, (r + 1) * 16)
                bank = mlp_bank(r, first, 0)
                for s in range(QUADS):
                    last = nc.tensor.transpose(bank[:, s * P:(s + 1) * P], bot[:, s, :], ident[:, :])
                last.then_inc(mlp_ready, 1)
                for t in range(TILES):
                    for g, features in enumerate(GROUPS):
                        n = t * NGR + g
                        pe.wait_ge(gathered[t][g], (r + 1) * 16 * len(features))
                        if not first or n >= 2:
                            per = (NGR * TILES) // 2
                            pe.wait_ge(evac_dve if n % 2 == 0 else evac_act, r * per + n // 2)
                        for j, f in enumerate(features):
                            last = nc.tensor.transpose(tp[:, n % 2, j * P:(j + 1) * P], emb[:, t, f, :], ident[:, :])
                        last.then_inc(transposed, 1)
                    a, b = evacs_until((t + 1) * NGR)
                    pe.wait_ge(evac_dve, r * (NGR * TILES // 2) + a)
                    pe.wait_ge(evac_act, r * (NGR * TILES // 2) + b)
                    v = embT[:, t % 2, :, :].rearrange("d (q s) f -> d q s f", s=QUADS)
                    for u in range(SPANS):
                        n = t * SPANS + u
                        if not first or n >= 2:
                            pe.wait_ge(extracted_dve if n % 2 == 0 else extracted_act, r * EXTRACTS + n // 2)
                        for j in range(SPAN):
                            q = u * SPAN + j
                            last = nc.tensor.matmul(gram[:, n % 2, j, 0:QUADS * NG], v[:, q, :, :].rearrange("d s f -> d (s f)"), v[:, q, :, 0:NG],
                                                    start=True, stop=True)
                        last.then_inc(grammed, 1)
                pe.wait_ge(packs_loaded, (r + 1) * 16 * len(PACKS))
                pe.wait_ge(mlp_evac, r * MLP_STEPS + 1)
                for m in range(M1):
                    bank = mlp_bank(r, first, 1 + m) if m else mlp[:, 1, :]
                    for c, k in enumerate(PAIR_ROWS):
                        nc.tensor.matmul(bank, w1[0:k, c, m * P:(m + 1) * P], packed[0:k, c, :], start=(c == 0), stop=False)
                    nc.tensor.matmul(bank, w1_bot[:, 2, m * P:(m + 1) * P], botT[:, :], start=False, stop=True).then_inc(mlp_ready, 1)
                for m in range(M2):
                    bank = mlp_bank(r, first, 1 + M1 + m)
                    for c in range(M1):
                        if m == 0 and c > M1 - 2:
                            pe.wait_ge(mlp_evac, r * MLP_STEPS + 2 + c)
                        last = nc.tensor.matmul(bank, w2[:, c, m * P:(m + 1) * P], h1[:, c, :], start=(c == 0), stop=(c == M1 - 1))
                    last.then_inc(mlp_ready, 1)
                bank = mlp_bank(r, first, 1 + M1 + M2)
                for c in range(M2):
                    if c > M2 - 2:
                        pe.wait_ge(mlp_evac, r * MLP_STEPS + 2 + M1 + c)
                    last = nc.tensor.matmul(bank[0:1, :], w3[:, c:c + 1], h2[:, c, :], start=(c == 0), stop=(c == M2 - 1))
                last.then_inc(mlp_ready, 1)
            rounds(pe, body)

        def evacuate(eng, copy, done, r, first, t, g):
            n = t * NGR + g
            eng.wait_ge(transposed, r * TILES * NGR + n + 1)
            if (not first or t >= 2) and g < 2:
                eng.wait_ge(grammed, (r * TILES + t - 1) * SPANS)
            f = GROUPS[g]
            dst = embT[:, t % 2, :, f[0]:f[0] + len(f)].rearrange("d b f -> d f b")
            copy(dst, tp[:, n % 2, 0:len(f) * P].rearrange("d (f b) -> d f b", b=P)).then_inc(done, 1)

        def extract(eng, copy, done, r, first, t, u):
            n = t * SPANS + u
            eng.wait_ge(grammed, r * TILES * SPANS + n + 1)
            if not first and t == 0:
                eng.wait_ge(stored, r * 16 * QUADS)
            for s in range(QUADS):
                own = slice(QS * s, QS * (s + 1))
                at = t * QS + u * SPAN
                last = copy(inter[own, :, at:at + SPAN],
                            gram[own, n % 2, :, s * NG:(s + 1) * NG].rearrange("f j g -> f g j"))
            last.then_inc(done, 1)

        @block.vector
        def _(dve):
            dve.memset(embT[:, :, :, NF:QS], 0.0).then_inc(pads_zeroed, 1)
            dve.memset(ids_all[:, ROUNDS * TILES:, :], 0).then_inc(pads_zeroed, 1)
            dve.wait_ge(weights_loaded, 16 * (CH + 6))
            dve.tensor_tensor(w1_bot[:, 2, :], w1_bot[:, 0, :], w1_bot[:, 1, :], ALU.add).then_inc(w1_bot_summed, 1)
            dve.wait_ge(ids_loaded, 16)
            dve.wait_ge(pads_zeroed, 2)

            def body(r, first):
                for t in range(TILES):
                    for g in range(NGR):
                        if evac_even(t, g):
                            evacuate(dve, nc.vector.tensor_copy, evac_dve, r, first, t, g)
                    dve.wait_ge(transposed, (r * TILES + t + 1) * NGR)
                    src = ids_all[:, TILES + t, :] if first else ids_all[:, bass.ds((r + 1) * TILES + t, 1), :].rearrange("p o f -> p (o f)")
                    nc.vector.tensor_copy(ids_now[:, t, :], src).then_inc(ids_ready, 1)
                    for u in range(SPANS):
                        if (t * SPANS + u) % 2 == 0:
                            extract(dve, nc.vector.tensor_copy, extracted_dve, r, first, t, u)
            rounds(dve, body)

        @block.scalar
        def _(act):
            for c, k in enumerate(PAIR_ROWS):
                act.dma_start(w1[0:k, c, :], w_top1[D + c * P:D + c * P + k, :]).then_inc(weights_loaded, 16)
            act.dma_start(w1_bot[:, 0, :], w_top1[0:D, :]).then_inc(weights_loaded, 16)
            act.dma_start(w1_bot[:, 1, :], w_top1[D + PAIRS:, :]).then_inc(weights_loaded, 16)
            act.dma_start(w2[:, :, :], w_top2.rearrange("(c p) n -> p c n", p=P)).then_inc(weights_loaded, 16)
            with nc.allow_non_contiguous_dma(reason="a few hundred elements"):
                act.dma_start(w3[:, :], w_top3.rearrange("(c p) one -> p (c one)", p=P)).then_inc(weights_loaded, 16)
                act.dma_start(b1[:, :], b_top1.rearrange("(c p) -> p c", p=P)).then_inc(weights_loaded, 16)
                act.dma_start(b2[:, :], b_top2.rearrange("(c p) -> p c", p=P)).then_inc(weights_loaded, 16)
            act.wait_ge(weights_loaded, 16 * (CH + 6))
            act.wait_ge(pads_zeroed, 2)

            def body(r, first):
                act.wait_ge(mlp_ready, r * MLP_STEPS + 1)
                act.copy(botT[:, :], mlp[:, 0, :]).then_inc(mlp_evac, 1)
                for t in range(TILES):
                    for g in range(NGR):
                        if not evac_even(t, g):
                            evacuate(act, nc.scalar.copy, evac_act, r, first, t, g)
                    for u in range(SPANS):
                        if (t * SPANS + u) % 2 == 1:
                            extract(act, nc.scalar.copy, extracted_act, r, first, t, u)
                act.wait_ge(stored, (r + 1) * 16 * QUADS)
                src = grams[r] if first else grams[bass.ds(r, 1)].rearrange("o f g n -> (o f) g n")
                for f, g, n, c, k in PACKS[N_PACK_A:]:
                    act.dma_start(packed[k:k + n, c, :], src[f, g:g + n, :]).then_inc(packs_loaded, 16)
                n = 1
                for h, b, blocks in ((h1, b1, M1), (h2, b2, M2)):
                    for m in range(blocks):
                        act.wait_ge(mlp_ready, r * MLP_STEPS + n + 1)
                        nc.scalar.activation(h[:, m, :], mlp[:, n % 2, :], ACT.Relu, bias=b[:, m:m + 1]).then_inc(mlp_evac, 1)
                        n += 1
                act.wait_ge(mlp_ready, r * MLP_STEPS + n + 1)
                if not first:
                    act.wait_ge(y_stored, r * 16)
                nc.scalar.copy(y[:, :], mlp[0:1, n % 2, :]).then_inc(mlp_evac, 1)
            rounds(act, body)


_OUTS = [((2048, 1), 'float32')]
NF = 27


def kernel(**inputs):
    import numpy as _np
    import concourse.bacc as _bacc
    from concourse import mybir as _mybir
    from concourse.bass_utils import run_bass_kernel_spmd as _run

    nc = _bacc.Bacc("TRN2", target_bir_lowering=False, num_devices=1)
    arrays = {}

    def take(name, a):
        a = _np.ascontiguousarray(a)
        arrays[f"in_{name}"] = a
        return nc.dram_tensor(f"in_{name}", a.shape, _mybir.dt.from_np(a.dtype), kind="ExternalInput").ap()

    ids = _np.asarray(inputs["ids"])
    ids = ids.reshape(-1, QUADS, TILES, QS, NF).transpose(0, 2, 3, 1, 4).reshape(ids.shape)
    bottom = take("bottom", inputs["r_bottom_mlp_out"])
    ids = take("ids", ids)
    tables = [take(f"tbl_{f}", inputs[f"tbl_{f}"]) for f in range(NF)]
    rest = [take(n, inputs[n]) for n in ("W_top1", "b_top1", "W_top2", "b_top2", "W_top3")]
    out = nc.dram_tensor("out_0", (bottom.shape[0], 1), F32, kind="ExternalOutput").ap()
    dlrm_tower(nc, bottom, ids, tables, *rest, out)
    r = _run(nc, [arrays], core_ids=[0])
    return r.results[0]["out_0"]
```

```python
from contextlib import ExitStack

import concourse.bass as bass
from concourse import mybir

F32 = mybir.dt.float32
F32R = mybir.dt.float32r
I32 = mybir.dt.int32
U32 = mybir.dt.uint32
ALU = mybir.AluOpType
ACT = mybir.ActivationFunctionType

P = 128
QUADS = 4
QS = P // QUADS
TILES = 4
ROUND = TILES * P
HALF = ROUND // 2
BANK = 512
GROUP = BANK // P
PAIR = BANK // HALF
SPAN = 8
SELECTED = 8
OH_RING = 4
STAGE = 3


def table_chunks(rows):
    chunks = -(-rows // P)
    while rows % chunks:
        chunks += 1
    return rows // chunks, chunks


def dlrm_tower(nc, bottom, ids, sel_ids, gather_tables, select_tables, w_top1, b_top1, w_top2, b_top2, w_top3, out):
    B, D = bottom.shape
    NGA, NSEL = len(gather_tables), len(select_tables)
    NF = NGA + NSEL
    ROUNDS = B // ROUND
    PAIRS = NF * (NF - 1) // 2
    NG = NF - 1
    H1, H2 = w_top1.shape[1], w_top2.shape[1]
    M1, M2 = H1 // P, H2 // P
    assert D == P and w_top1.shape[0] == D + PAIRS + D and NF <= QS and NSEL % PAIR == 0
    GROUPS = [list(range(a, min(a + GROUP, NGA))) for a in range(0, NGA, GROUP)]
    NGR = len(GROUPS)
    SEL_PAIRS = NSEL // PAIR
    K, CHUNKS = table_chunks(select_tables[0].shape[0])
    assert K <= P and all(t.shape == select_tables[0].shape for t in select_tables)
    PAIR_ROWS = [min(P, PAIRS - a) for a in range(0, PAIRS, P)]
    CH = len(PAIR_ROWS)
    SPANS = QS // SPAN
    PACKS = []
    for f in range(1, NF):
        k, g = f * (f - 1) // 2, 0
        while g < f:
            n = min(f - g, P - k % P)
            PACKS.append((f, g, n, k // P, k % P))
            k, g = k + n, g + n
    MLP_STEPS = 1 + M1 + M2 + 1
    assert MLP_STEPS % 2 == 0

    STEPS = [("select", j) for j in range(SEL_PAIRS - 1)] + [("rows", 0), ("select", SEL_PAIRS - 1)]
    STEPS += [("gram", 0, 0), ("gram", 0, 1), ("rows", 1)] + [("gram", 0, u) for u in range(2, SPANS)]
    STEPS += [("gram", 1, u) for u in range(SPANS)]
    FT_HALF = SEL_PAIRS + 2 * NGR
    GRAM_HALF = 2 * SPANS
    assert FT_HALF % 2 == 0

    def numbered(steps):
        ft = gr = 0
        for step in steps:
            if step[0] == "gram":
                yield step, gr
                gr += 1
            else:
                yield step, ft
                ft += NGR if step[0] == "rows" else 1

    HALF_STEPS = list(numbered(STEPS))
    FT_NEEDED = [next(n for s, n in HALF_STEPS if s == ("rows", 1)), FT_HALF]

    def span_is_dve(n):
        return n % 2 == 0

    DVE_SPANS = sum(span_is_dve(n) for n in range(GRAM_HALF))
    ACT_SPANS = GRAM_HALF - DVE_SPANS

    ids_v = ids.rearrange("(n p) f -> p n f", p=P)
    bottom_v = bottom.rearrange("(r s p) d -> r p s d", s=QUADS, p=P)
    out_v = out.rearrange("(r n) one -> r one n", n=ROUND)
    grams = nc.dram_tensor("grams", [ROUNDS, NF, NG, ROUND], F32, kind="Internal").ap()

    with ExitStack() as ctx:
        def sb(name, shape, dt=F32):
            return ctx.enter_context(nc.sbuf_tensor(name, shape, dt))

        def psum(name, shape):
            return ctx.enter_context(nc.psum_tensor(name, shape, F32))

        def sem(name):
            return ctx.enter_context(nc.semaphore(name))

        ident = sb("ident", [P, P])
        row_id = sb("row_id", [P, CHUNKS], I32)
        row_idf = sb("row_idf", [P, CHUNKS])
        ids_all = sb("ids_all", [P, (ROUNDS + 1) * TILES, NGA], I32)
        ids_now = sb("ids_now", [P, TILES, NGA], I32)
        ids_bc = sb("ids_bc", [P, NSEL, HALF], I32)
        onehot = sb("onehot", [P, OH_RING, PAIR * HALF], F32R)
        tab_hi = sb("tab_hi", [P, NSEL, CHUNKS, D], F32R)
        tab_lo = sb("tab_lo", [P, NSEL, CHUNKS, D], F32R)
        emb = sb("emb", [P, TILES, NGA, D])
        embT = sb("embT", [P, 2, P, QS])
        inter = sb("inter", [P, NG, P])
        packed = sb("packed", [P, CH, ROUND])
        bot = sb("bot", [P, QUADS, D])
        botT = sb("botT", [P, ROUND])
        w1 = sb("w1", [P, CH + 1, H1])
        w2 = sb("w2", [P, M1, H2])
        w3 = sb("w3", [P, M2])
        b1 = sb("b1", [P, M1])
        b2 = sb("b2", [P, M2])
        h1 = sb("h1", [P, M1, ROUND])
        h2 = packed[:, 0:M2, :]
        y = botT[0:1, :]
        stage = inter[:, :, :].rearrange("p g n -> p (g n)")[:, 0:STAGE * CHUNKS * D].rearrange(
            "p (i n) -> p i n", i=STAGE)

        ft = psum("ft", [P, 2, BANK])
        gram = psum("gram", [P, 2, SPAN, P])
        mlp = psum("mlp", [P, 2, BANK])

        N_WEIGHTS = 16 * (CH + 6)
        weights_loaded = sem("weights_loaded")
        w1_bot_summed = sem("w1_bot_summed")
        table_staged = [sem(f"table_staged_{i}") for i in range(STAGE)]
        table_hi = sem("table_hi")
        table_lo = sem("table_lo")
        ids_loaded = sem("ids_loaded")
        ids_ready = sem("ids_ready")
        ids_bc_loaded = sem("ids_bc_loaded")
        slots_taken = sem("slots_taken")
        ident_zeroed = sem("ident_zeroed")
        ident_ready = sem("ident_ready")
        row_id_ready = sem("row_id_ready")
        row_idf_ready = sem("row_idf_ready")
        pads_zeroed = sem("pads_zeroed")
        gathered = [[sem(f"gathered_{t}_{g}") for g in range(NGR)] for t in range(TILES)]
        onehot_ready = sem("onehot_ready")
        onehot_used = sem("onehot_used")
        rows_ready = sem("rows_ready")
        ft_dve = sem("ft_dve")
        ft_act = sem("ft_act")
        grammed = sem("grammed")
        extracted_dve = sem("extracted_dve")
        extracted_act = sem("extracted_act")
        stored = sem("stored")
        packs_loaded = sem("packs_loaded")
        packs_pool = sem("packs_pool")
        bot_loaded = sem("bot_loaded")
        mlp_ready = sem("mlp_ready")
        mlp_evac = sem("mlp_evac")
        y_stored = sem("y_stored")

        block = ctx.enter_context(nc.Block())

        def rounds(eng, body, last):
            body(0, True)
            with eng.Fori(1, ROUNDS) as r:
                body(r, False)
            last(ROUNDS - 1)

        def row(ap, r):
            if isinstance(r, int):
                return ap[r]
            names = " ".join("abcd"[:len(ap.shape) - 1])
            first = names.split()[0]
            return ap[bass.ds(r, 1)].rearrange(f"o {names} -> (o {first}) {names[2:]}")

        def load_packs(eng, src, packs, loaded):
            for f, g, n, c, k in packs:
                eng.dma_start(packed[k:k + n, c, :], src[f, g:g + n, :]).then_inc(loaded, 16)

        @block.sync
        def _(sp):
            sp.dma_start(ids_all[:, 0:ROUNDS * TILES, :], ids_v).then_inc(ids_loaded, 16)

            def load_ids_bc(half):
                src = row(sel_ids, half)
                sp.dma_start(ids_bc[:, :, :], src.to_broadcast([P, NSEL, HALF])).then_inc(ids_bc_loaded, 16)

            load_ids_bc(0)
            for i, table in enumerate(select_tables):
                if i >= STAGE:
                    sp.wait_ge(table_lo, i - STAGE + 1)
                sp.dma_start(stage[0:K, i % STAGE, :], table.rearrange("(p c) d -> p (c d)", c=CHUNKS)).then_inc(table_staged[i % STAGE], 16)

            def finish(r, packs):
                sp.dma_start(bot[:, :, :], row(bottom_v, r)).then_inc(bot_loaded, 16)
                sp.wait_ge(extracted_dve, (r + 1) * 2 * DVE_SPANS)
                sp.wait_ge(extracted_act, (r + 1) * 2 * ACT_SPANS)
                dst = row(grams, r)
                for s in range(QUADS):
                    sp.dma_start(dst[:, :, s * P:(s + 1) * P], inter[QS * s:QS * s + NF, :, :]).then_inc(stored, 16)
                sp.wait_ge(stored, (r + 1) * 16 * QUADS)
                load_packs(sp, dst, packs, packs_loaded)

            def store_y(r):
                sp.wait_ge(mlp_evac, (r + 1) * MLP_STEPS)
                sp.dma_start(row(out_v, r), y).then_inc(y_stored, 16)
                sp.wait_ge(y_stored, (r + 1) * 16)

            def body(r, first):
                if not first:
                    finish(r - 1, PACKS)
                sp.wait_ge(onehot_ready, (2 * r + 1) * SEL_PAIRS * CHUNKS)
                load_ids_bc(2 * r + 1)
                if not first:
                    store_y(r - 1)
                sp.wait_ge(onehot_ready, (2 * r + 2) * SEL_PAIRS * CHUNKS)
                load_ids_bc(2 * r + 2)

            def last(r):
                finish(r, PACKS[0::3])
                store_y(r)
            rounds(sp, body, last)
            sp.wait_ge(ids_bc_loaded, 16 * (2 * ROUNDS + 1))

        @block.gpsimd
        def _(pool):
            pool.memset(ident[:, :], 0.0).then_inc(ident_zeroed, 1)
            pool.iota(row_id[:, :], pattern=[[1, CHUNKS]], base=0, channel_multiplier=CHUNKS).then_inc(row_id_ready, 1)
            pool.wait_ge(ident_zeroed, 1)
            pool.affine_select(out=ident[:, :], in_=ident[:, :], compare_op=ALU.not_equal, fill=1.0,
                               base=0, pattern=[[-1, P]], channel_multiplier=1).then_inc(ident_ready, 1)
            pool.wait_ge(ids_loaded, 16)

            def body(r, first):
                for t in range(TILES):
                    if not first:
                        pool.wait_ge(ids_ready, (r - 1) * TILES + t + 1)
                        pool.wait_ge(rows_ready, ((r - 1) * TILES + t + 1) * NGR)
                        pool.sem_inc(slots_taken, 1)
                    idx = ids_all if first else ids_now
                    for g, features in enumerate(GROUPS):
                        for f in features:
                            pool.indirect_dma_start(
                                out=emb[:, t, f, :], out_offset=None, in_=gather_tables[f],
                                in_offset=bass.IndirectOffsetOnAxis(ap=idx[:, t, f:f + 1].bitcast(U32), axis=0),
                            ).then_inc(gathered[t][g], 16)

            def last(r):
                pool.wait_ge(mlp_ready, r * MLP_STEPS)
                pool.wait_ge(stored, (r + 1) * 16 * QUADS)
                load_packs(pool, grams[r], PACKS[1::3], packs_pool)
            rounds(pool, body, last)

        @block.tensor
        def _(pe):
            def bank_copied(r, first, h, n):
                if not first or h or n >= 2:
                    pe.wait_ge(ft_dve if n % 2 == 0 else ft_act, (2 * r + h) * (FT_HALF // 2) + n // 2)

            def select(r, first, h, j, n):
                bank_copied(r, first, h, n)
                for c in range(CHUNKS):
                    at = j * CHUNKS + c
                    pe.wait_ge(onehot_ready, (2 * r + h) * SEL_PAIRS * CHUNKS + at + 1)
                    for i in range(PAIR):
                        if first and h == 0 and c == 0:
                            pe.wait_ge(table_lo, PAIR * j + i + 1)
                        cols = slice(i * HALF, (i + 1) * HALF)
                        for part in (tab_hi, tab_lo):
                            mm = nc.tensor.matmul(ft[:, n % 2, cols], part[0:K, PAIR * j + i, c, :],
                                                  onehot[0:K, at % OH_RING, cols],
                                                  start=(c == 0 and i == 0 and part is tab_hi),
                                                  stop=(c == CHUNKS - 1 and part is tab_lo), skip_group_check=True)
                    mm.then_inc(onehot_used, 1)

            def rows(r, first, h, i, n):
                t = 2 * h + i
                for g, features in enumerate(GROUPS):
                    pe.wait_ge(gathered[t][g], (r + 1) * 16 * len(features))
                    bank_copied(r, first, h, n + g)
                    for j, f in enumerate(features):
                        last = nc.tensor.transpose(ft[:, (n + g) % 2, j * P:(j + 1) * P], emb[:, t, f, :], ident[:, :])
                    last.then_inc(rows_ready, 1)

            def products(r, first, h, i, u, n):
                if u == 0:
                    need = FT_NEEDED[i]
                    pe.wait_ge(ft_dve, (2 * r + h) * (FT_HALF // 2) + (need + 1) // 2)
                    pe.wait_ge(ft_act, (2 * r + h) * (FT_HALF // 2) + need // 2)
                if not first or h or n >= 2:
                    m = n - 2 + (GRAM_HALF if n < 2 else 0)
                    before = (2 * r + h) - (1 if n < 2 else 0)
                    done = sum(span_is_dve(x) == span_is_dve(m) for x in range(m + 1))
                    if span_is_dve(m):
                        pe.wait_ge(extracted_dve, before * DVE_SPANS + done)
                    else:
                        pe.wait_ge(extracted_act, before * ACT_SPANS + done)
                for j in range(SPAN):
                    a = (u * SPAN + j) * QUADS
                    four = embT[:, i, a:a + QUADS, :]
                    last = nc.tensor.matmul(gram[:, n % 2, j, 0:QUADS * NG], four.rearrange("d s f -> d (s f)"),
                                            four[:, :, 0:NG], start=True, stop=True)
                last.then_inc(grammed, 1)

            def mlp_bank(r, n):
                pe.wait_ge(mlp_evac, r * MLP_STEPS + n - 1)
                return mlp[:, n % 2, :]

            def top(r, packs, pool_packs):
                pe.wait_ge(weights_loaded, N_WEIGHTS)
                pe.wait_ge(w1_bot_summed, 1)
                pe.wait_ge(bot_loaded, (r + 1) * 16)
                bank = mlp[:, 0, :]
                for s in range(QUADS):
                    last = nc.tensor.transpose(bank[:, s * P:(s + 1) * P], bot[:, s, :], ident[:, :])
                last.then_inc(mlp_ready, 1)
                pe.wait_ge(packs_loaded, r * 16 * len(PACKS) + 16 * len(packs))
                if pool_packs:
                    pe.wait_ge(packs_pool, 16 * len(pool_packs))
                pe.wait_ge(mlp_evac, r * MLP_STEPS + 1)
                for m in range(M1):
                    bank = mlp_bank(r, 1 + m) if m else mlp[:, 1, :]
                    cols = slice(m * P, (m + 1) * P)
                    for c, k in enumerate(PAIR_ROWS):
                        nc.tensor.matmul(bank, w1[0:k, c, cols], packed[0:k, c, :], start=(c == 0), stop=False)
                    nc.tensor.matmul(bank, w1[:, CH, cols], botT[:, :], start=False, stop=True).then_inc(mlp_ready, 1)
                for m in range(M2):
                    bank = mlp_bank(r, 1 + M1 + m)
                    for c in range(M1):
                        if m == 0 and c > M1 - 2:
                            pe.wait_ge(mlp_evac, r * MLP_STEPS + 2 + c)
                        last = nc.tensor.matmul(bank, w2[:, c, m * P:(m + 1) * P], h1[:, c, :], start=(c == 0), stop=(c == M1 - 1))
                    last.then_inc(mlp_ready, 1)
                bank = mlp_bank(r, 1 + M1 + M2)
                for c in range(M2):
                    if c > M2 - 2:
                        pe.wait_ge(mlp_evac, r * MLP_STEPS + 2 + M1 + c)
                    last = nc.tensor.matmul(bank[0:1, :], w3[:, c:c + 1], h2[:, c, :], start=(c == 0), stop=(c == M2 - 1))
                last.then_inc(mlp_ready, 1)

            pe.wait_ge(ident_ready, 1)

            def body(r, first):
                for h in range(2):
                    for step, n in HALF_STEPS:
                        if step[0] == "select":
                            select(r, first, h, step[1], n)
                        elif step[0] == "rows":
                            rows(r, first, h, step[1], n)
                        else:
                            products(r, first, h, step[1], step[2], n)
                    if h == 0 and not first:
                        top(r - 1, PACKS, [])
            rounds(pe, body, lambda r: top(r, PACKS[0::3] + PACKS[2::3], PACKS[1::3]))

        def ft_copy(eng, copy, done, r, first, h, dst, src):
            if not first or h:
                eng.wait_ge(grammed, (2 * r + h) * GRAM_HALF)
            copy(dst, src).then_inc(done, 1)

        def ft_copies(eng, copy, done, parity, r, first, h, step, n):
            if step[0] == "select":
                if n % 2 == parity:
                    f = NGA + PAIR * step[1]
                    eng.wait_ge(onehot_used, ((2 * r + h) * SEL_PAIRS + step[1] + 1) * CHUNKS)
                    ft_copy(eng, copy, done, r, first, h,
                            embT[:, :, :, f:f + PAIR].rearrange("d i b f -> d f (i b)"),
                            ft[:, n % 2, :].rearrange("d (f b) -> d f b", b=HALF))
                return
            for g, features in enumerate(GROUPS):
                if (n + g) % 2 == parity:
                    f, k = features[0], len(features)
                    eng.wait_ge(rows_ready, (r * TILES + 2 * h + step[1]) * NGR + g + 1)
                    ft_copy(eng, copy, done, r, first, h,
                            embT[:, step[1], :, f:f + k].rearrange("d b f -> d f b"),
                            ft[:, parity, 0:k * P].rearrange("d (f b) -> d f b", b=P))

        def extract(eng, copy, done, r, first, h, i, u, n):
            eng.wait_ge(grammed, (2 * r + h) * GRAM_HALF + n + 1)
            if not first and h == 0:
                eng.wait_ge(stored, r * 16 * QUADS)
            at = (2 * h + i) * QS + u * SPAN
            for s in range(QUADS):
                own = slice(QS * s, QS * (s + 1))
                last = copy(inter[own, :, at:at + SPAN],
                            gram[own, n % 2, :, s * NG:(s + 1) * NG].rearrange("f j g -> f g j"))
            last.then_inc(done, 1)

        @block.vector
        def _(dve):
            dve.wait_ge(row_id_ready, 1)
            nc.vector.tensor_copy(row_idf[:, :], row_id[:, :]).then_inc(row_idf_ready, 1)
            dve.memset(ids_all[:, ROUNDS * TILES:, :], 0).then_inc(pads_zeroed, 1)
            dve.memset(embT[:, :, :, NF:QS], 0.0).then_inc(pads_zeroed, 1)
            dve.wait_ge(pads_zeroed, 2)
            dve.wait_ge(row_idf_ready, 1)

            def split(i):
                dve.wait_ge(table_hi, i + 1)
                nc.vector.tensor_tensor(tab_lo[0:K, i, :, :].rearrange("p c d -> p (c d)"), stage[0:K, i % STAGE, :],
                                        tab_hi[0:K, i, :, :].rearrange("p c d -> p (c d)").bitcast(F32), ALU.subtract).then_inc(table_lo, 1)

            def onehots(r, first, h, j, chunks):
                dve.wait_ge(ids_bc_loaded, (2 * r + h + 1) * 16)
                for c in chunks:
                    at = j * CHUNKS + c
                    if not first or h or at >= OH_RING:
                        dve.wait_ge(onehot_used, (2 * r + h) * SEL_PAIRS * CHUNKS + at - OH_RING + 1)
                    nc.vector.tensor_scalar(onehot[0:K, at % OH_RING, :],
                                            ids_bc[0:K, PAIR * j:PAIR * (j + 1), :].rearrange("p i n -> p (i n)"),
                                            row_idf[0:K, c:c + 1], None, ALU.is_equal).then_inc(onehot_ready, 1)

            for i in range(NSEL):
                split(i)
            dve.wait_ge(ids_loaded, 16)

            def body(r, first):
                for h in range(2):
                    onehots(r, first, h, 0, range(OH_RING))
                    for step, n in HALF_STEPS:
                        if step[0] == "select":
                            onehots(r, first, h, step[1], range(OH_RING, CHUNKS))
                            if step[1] + 1 < SEL_PAIRS:
                                onehots(r, first, h, step[1] + 1, range(OH_RING))
                        if step[0] == "gram":
                            if span_is_dve(n):
                                extract(dve, nc.vector.tensor_copy, extracted_dve, r, first, h, step[1], step[2], n)
                        else:
                            ft_copies(dve, nc.vector.tensor_copy, ft_dve, 0, r, first, h, step, n)
                        if step[0] == "rows":
                            t = 2 * h + step[1]
                            dve.wait_ge(rows_ready, (r * TILES + t + 1) * NGR)
                            src = ids_all[:, TILES + t, :] if first else ids_all[:, bass.ds((r + 1) * TILES + t, 1), :].rearrange("p o f -> p (o f)")
                            nc.vector.tensor_copy(ids_now[:, t, :], src).then_inc(ids_ready, 1)
                    if h == 0 and first:
                        dve.wait_ge(weights_loaded, N_WEIGHTS)
                        nc.vector.tensor_tensor(w1[:, CH, :], h1[:, 0, :], h1[:, 1, :], ALU.add).then_inc(w1_bot_summed, 1)
            rounds(dve, body, lambda r: None)

        @block.scalar
        def _(act):
            for c, k in enumerate(PAIR_ROWS):
                act.dma_start(w1[0:k, c, :], w_top1[D + c * P:D + c * P + k, :]).then_inc(weights_loaded, 16)
            act.dma_start(h1[:, 0, :], w_top1[0:D, :]).then_inc(weights_loaded, 16)
            act.dma_start(h1[:, 1, :], w_top1[D + PAIRS:, :]).then_inc(weights_loaded, 16)
            act.dma_start(w2[:, :, :], w_top2.rearrange("(c p) n -> p c n", p=P)).then_inc(weights_loaded, 16)
            with nc.allow_non_contiguous_dma(reason="a few hundred elements"):
                act.dma_start(w3[:, :], w_top3.rearrange("(c p) one -> p (c one)", p=P)).then_inc(weights_loaded, 16)
                act.dma_start(b1[:, :], b_top1.rearrange("(c p) -> p c", p=P)).then_inc(weights_loaded, 16)
                act.dma_start(b2[:, :], b_top2.rearrange("(c p) -> p c", p=P)).then_inc(weights_loaded, 16)
            for i in range(NSEL):
                act.wait_ge(table_staged[i % STAGE], 16 * (i // STAGE + 1))
                nc.scalar.copy(tab_hi[0:K, i, :, :].rearrange("p c d -> p (c d)"), stage[0:K, i % STAGE, :]).then_inc(table_hi, 1)
            act.wait_ge(pads_zeroed, 2)
            act.wait_ge(table_lo, NSEL)

            def top(r):
                act.wait_ge(mlp_ready, r * MLP_STEPS + 1)
                act.copy(botT[:, :], mlp[:, 0, :]).then_inc(mlp_evac, 1)
                n = 1
                for h, b, blocks in ((h1, b1, M1), (h2, b2, M2)):
                    for m in range(blocks):
                        act.wait_ge(mlp_ready, r * MLP_STEPS + n + 1)
                        nc.scalar.activation(h[:, m, :], mlp[:, n % 2, :], ACT.Relu, bias=b[:, m:m + 1]).then_inc(mlp_evac, 1)
                        n += 1
                act.wait_ge(mlp_ready, r * MLP_STEPS + n + 1)
                nc.scalar.copy(y, mlp[0:1, n % 2, :]).then_inc(mlp_evac, 1)

            def body(r, first):
                for h in range(2):
                    for step, n in HALF_STEPS:
                        if step[0] != "gram":
                            ft_copies(act, nc.scalar.copy, ft_act, 1, r, first, h, step, n)
                        elif not span_is_dve(n):
                            extract(act, nc.scalar.copy, extracted_act, r, first, h, step[1], step[2], n)
                    if h == 0 and not first:
                        top(r - 1)

            def last(r):
                act.wait_ge(stored, (r + 1) * 16 * QUADS)
                load_packs(act, grams[r], PACKS[2::3], packs_loaded)
                top(r)
            rounds(act, body, last)


NF = 27
D = 128


def kernel(**inputs):
    import numpy as _np
    import concourse.bacc as _bacc
    from concourse import mybir as _mybir
    from concourse.bass_utils import run_bass_kernel_spmd as _run

    nc = _bacc.Bacc("TRN2", target_bir_lowering=False, num_devices=1)
    arrays = {}

    def take(name, a):
        a = _np.ascontiguousarray(a)
        arrays[f"in_{name}"] = a
        return nc.dram_tensor(f"in_{name}", a.shape, _mybir.dt.from_np(a.dtype), kind="ExternalInput").ap()

    by_rows = sorted(range(NF), key=lambda f: (inputs[f"tbl_{f}"].shape[0], f))
    selected = sorted(by_rows[:SELECTED])
    gathered = sorted(by_rows[SELECTED:])
    order = gathered + selected
    w = _np.asarray(inputs["W_top1"])
    pairs = [(max(order[f], order[g]), min(order[f], order[g])) for f in range(NF) for g in range(f)]
    at = [D + a * (a - 1) // 2 + b for a, b in pairs]
    w = _np.concatenate([w[:D], w[_np.array(at)], w[D + len(at):]])
    ids = _np.asarray(inputs["ids"])
    ids = ids.reshape(-1, QUADS, TILES, QS, NF).transpose(0, 2, 3, 1, 4).reshape(ids.shape)
    sel_ids = ids[:, selected].reshape(-1, HALF, SELECTED).transpose(0, 2, 1)
    sel_ids = _np.concatenate([sel_ids, _np.zeros_like(sel_ids[:1])])[:, None]

    args = [take("bottom", inputs["r_bottom_mlp_out"]), take("ids", ids[:, gathered]), take("sel_ids", sel_ids),
            [take(f"tbl_{f}", inputs[f"tbl_{f}"]) for f in gathered],
            [take(f"tbl_{f}", inputs[f"tbl_{f}"]) for f in selected], take("W_top1", w)]
    args += [take(n, inputs[n]) for n in ("b_top1", "W_top2", "b_top2", "W_top3")]
    out = nc.dram_tensor("out_0", (ids.shape[0], 1), F32, kind="ExternalOutput").ap()
    dlrm_tower(nc, *args, out)
    r = _run(nc, [arrays], core_ids=[0])
    return r.results[0]["out_0"]
```

```python
from contextlib import ExitStack

import concourse.bass as bass
from concourse import mybir

F32 = mybir.dt.float32
F32R = mybir.dt.float32r
I32 = mybir.dt.int32
U32 = mybir.dt.uint32
ALU = mybir.AluOpType
ACT = mybir.ActivationFunctionType

P = 128
QUADS = 4
QS = P // QUADS
TILES = 4
ROUND = TILES * P
HALF = ROUND // 2
BANK = 512
GROUP = BANK // P
PAIR = BANK // HALF
SPAN = 8
SELECTED = 8
OH_RING = 4
STAGE = 3


def table_chunks(rows):
    chunks = -(-rows // P)
    while rows % chunks:
        chunks += 1
    return rows // chunks, chunks


def dlrm_tower(nc, bottom, ids, sel_ids, gather_tables, select_tables, w_top1, b_top1, w_top2, b_top2, w_top3, out):
    B, D = bottom.shape
    NGA, NSEL = len(gather_tables), len(select_tables)
    NF = NGA + NSEL
    ROUNDS = B // ROUND
    PAIRS = NF * (NF - 1) // 2
    NG = NF - 1
    H1, H2 = w_top1.shape[1], w_top2.shape[1]
    M1, M2 = H1 // P, H2 // P
    assert D == P and w_top1.shape[0] == D + PAIRS + D and NF <= QS and NSEL % PAIR == 0
    GROUPS = [list(range(a, min(a + GROUP, NGA))) for a in range(0, NGA, GROUP)]
    NGR = len(GROUPS)
    SEL_PAIRS = NSEL // PAIR
    K, CHUNKS = table_chunks(select_tables[0].shape[0])
    assert K <= P and all(t.shape == select_tables[0].shape for t in select_tables)
    PAIR_ROWS = [min(P, PAIRS - a) for a in range(0, PAIRS, P)]
    CH = len(PAIR_ROWS)
    SPANS = QS // SPAN
    PACKS = []
    for f in range(1, NF):
        k, g = f * (f - 1) // 2, 0
        while g < f:
            n = min(f - g, P - k % P)
            PACKS.append((f, g, n, k // P, k % P))
            k, g = k + n, g + n
    PACKS.sort(key=lambda pack: -pack[3])
    POOL_PACKS = PACKS[2::3]
    X_ORDER = [CH] + list(reversed(range(CH)))
    X_ROWS = PAIR_ROWS + [D]
    W1_SPLITS = 3
    assert CH == 3
    SP_PACKS = [pack for pack in PACKS if pack not in POOL_PACKS]
    MLP_STEPS = 1 + M1 + M2 + 1

    FEATURE_STEPS = [("select", j) for j in range(SEL_PAIRS)] + [("rows", 0), ("rows", 1)]
    FT_HALF = SEL_PAIRS + 2 * NGR
    ROWS_AT = [SEL_PAIRS, SEL_PAIRS + NGR]
    GRAM_HALF = 2 * SPANS
    BANKS = 4

    def results(r, h):
        if isinstance(r, int) and r == 0 and h == 0:
            return 0
        return 2 * r * (FT_HALF + MLP_STEPS) + h * (FT_HALF + MLP_STEPS) - MLP_STEPS

    assert 2 * FT_HALF % BANKS == 0 and MLP_STEPS % BANKS == 0
    HALF_BANK = [0, FT_HALF % BANKS]
    MLP_BANK = [HALF_BANK[1], HALF_BANK[0]]
    assert M1 == BANKS
    assert GRAM_HALF // 2 == OH_RING
    HALVES = 2 * ROUNDS
    QN = HALF // QUADS

    ids_v = ids.rearrange("(n p) f -> p n f", p=P)
    bottom_v = bottom.rearrange("(m b p) d -> m p b d", b=HALF // P, p=P)
    out_v = out.rearrange("(m n) one -> m one n", n=HALF)
    grams = nc.dram_tensor("grams", [HALVES, QUADS, QS, NG, QN], F32, kind="Internal").ap()

    with ExitStack() as ctx:
        def sb(name, shape, dt=F32):
            return ctx.enter_context(nc.sbuf_tensor(name, shape, dt))

        def psum(name, shape):
            return ctx.enter_context(nc.psum_tensor(name, shape, F32))

        def sem(name):
            return ctx.enter_context(nc.semaphore(name))

        ident = sb("ident", [P, P])
        row_id = sb("row_id", [P, CHUNKS], I32)
        row_idf = sb("row_idf", [P, CHUNKS])
        ids_all = sb("ids_all", [P, (ROUNDS + 1) * TILES, NGA], I32)
        ids_now = sb("ids_now", [P, TILES, NGA], I32)
        ids_bc = sb("ids_bc", [P, NSEL, HALF], I32)
        onehot = sb("onehot", [P, OH_RING, PAIR * HALF], F32R)
        tab_hi = sb("tab_hi", [P, NSEL, CHUNKS, D], F32R)
        tab_lo = sb("tab_lo", [P, NSEL, CHUNKS, D], F32R)
        emb = sb("emb", [P, TILES, NGA, D])
        embT = sb("embT", [P, 2, P, QS])
        inter = sb("inter", [P, NG, QN])
        packed = sb("packed", [P, 2, CH, HALF])
        bot = sb("bot", [P, 2, HALF // P, D])
        botT = sb("botT", [P, HALF])
        x_hi = sb("x_hi", [P, CH + 1, HALF], F32R)
        x_lo = sb("x_lo", [P, CH + 1, HALF], F32R)
        w1_hi = sb("w1_hi", [P, CH + 1, H1], F32R)
        w1_lo = sb("w1_lo", [P, CH + 1, H1], F32R)
        w2 = sb("w2", [P, M1, H2])
        w3 = sb("w3", [P, M2])
        b1 = sb("b1", [P, M1])
        b2 = sb("b2", [P, M2])
        h1 = sb("h1", [P, M1, HALF])
        h2 = sb("h2", [P, M2, HALF])
        y = bot[0:1, :, :, :].rearrange("p a b d -> p a (b d)")
        def flat(buffer, names):
            return buffer.rearrange(f"p {names} -> p ({names})")[:, 0:CHUNKS * D]
        bot_uses = sb("bot_uses", [P, 2, H1])
        stage = [flat(inter[:, :, :], "g n"), flat(packed[:, :, :, :], "a c n"), flat(bot_uses[:, :, :], "a n")]
        w1_raw = [h1.rearrange("p m n -> p (m n)").rearrange("p (c n) -> p c n", n=H1),
                  h2.rearrange("p (o m) n -> p o (m n)", o=1)]

        work = psum("work", [P, BANKS, BANK])
        gram = psum("gram", [P, 2, SPAN, P])

        N_WEIGHTS = 16 * (CH + 6)
        weights_loaded = sem("weights_loaded")
        w1_bot_summed = sem("w1_bot_summed")
        w1_hi_ready = sem("w1_hi_ready")
        w1_split = sem("w1_split")
        packed_hi_ready = sem("packed_hi_ready")
        packed_split = sem("packed_split")
        bottom_hi_ready = sem("bottom_hi_ready")
        bottom_split = sem("bottom_split")
        table_staged = [sem(f"table_staged_{i}") for i in range(STAGE)]
        table_hi = sem("table_hi")
        table_lo = sem("table_lo")
        ids_loaded = sem("ids_loaded")
        ids_ready = sem("ids_ready")
        ids_bc_loaded = sem("ids_bc_loaded")
        slots_taken = sem("slots_taken")
        ident_zeroed = sem("ident_zeroed")
        ident_ready = sem("ident_ready")
        row_id_ready = sem("row_id_ready")
        row_idf_ready = sem("row_idf_ready")
        pads_zeroed = sem("pads_zeroed")
        gathered = [[sem(f"gathered_{t}_{g}") for g in range(NGR)] for t in range(TILES)]
        onehot_ready = sem("onehot_ready")
        onehot_used = sem("onehot_used")
        rows_ready = sem("rows_ready")
        copied = sem("copied")
        grammed = sem("grammed")
        extracted_dve = sem("extracted_dve")
        extracted_act = sem("extracted_act")
        stored = sem("stored")
        packs_loaded = [[sem(f"packs_loaded_{par}_{c}") for c in range(CH)] for par in range(2)]
        packs_pool = [sem(f"packs_pool_{c}") for c in range(CH)]
        bot_loaded = [sem(f"bot_loaded_{par}") for par in range(2)]
        mlp_ready = sem("mlp_ready")
        y_stored = sem("y_stored")
        halves_out = sem("halves_out")

        block = ctx.enter_context(nc.Block())

        def rounds(eng, body, last):
            body(0, True)
            with eng.Fori(1, ROUNDS) as r:
                body(r, False)
            last(HALVES - 1)

        def row(ap, r):
            if isinstance(r, int):
                return ap[r]
            names = " ".join("abcd"[:len(ap.shape) - 1])
            first = names.split()[0]
            return ap[bass.ds(r, 1)].rearrange(f"o {names} -> (o {first}) {names[2:]}")

        def load_packs(eng, src, par, packs, pool=False):
            for f, g, n, c, k in packs:
                eng.dma_start(packed[k:k + n, par, c, :].rearrange("k (s n) -> k s n", s=QUADS),
                              src[:, f, g:g + n, :].rearrange("s k n -> k s n")).then_inc(packs_pool[c] if pool else packs_loaded[par][c], 16)

        def load_ids_bc(eng, half):
            src = row(sel_ids, half)
            eng.dma_start(ids_bc[:, :, :], src.to_broadcast([P, NSEL, HALF])).then_inc(ids_bc_loaded, 16)

        @block.sync
        def _(sp):
            sp.dma_start(ids_all[:, 0:ROUNDS * TILES, :], ids_v).then_inc(ids_loaded, 16)

            load_ids_bc(sp, 0)
            for i, table in enumerate(select_tables):
                if i >= STAGE:
                    sp.wait_ge(table_lo, i - STAGE + 1)
                for part in (slice(0, K // 16 * 16), slice(K // 16 * 16, K)):
                    sp.dma_start(stage[i % STAGE][part, :], table.rearrange("(p c) d -> p (c d)", c=CHUNKS)[part, :]).then_inc(table_staged[i % STAGE], 16)

            def finish(m, par, packs):
                sp.dma_start(bot[:, par, :, :], row(bottom_v, m)).then_inc(bot_loaded[par], 16)
                sp.wait_ge(extracted_dve, (m + 1) * (GRAM_HALF // 2))
                sp.wait_ge(extracted_act, (m + 1) * (GRAM_HALF // 2))
                dst = row(grams, m)
                sp.dma_start(dst.rearrange("s f g n -> (s f) g n"), inter[:, :, :]).then_inc(stored, 16)
                sp.wait_ge(stored, (m + 1) * 16)
                load_packs(sp, dst, par, packs)

            def store_y(m, par, results_then):
                sp.wait_ge(copied, results_then)
                sp.dma_start(row(out_v, m), y[:, par, :]).then_inc(y_stored, 16)
                sp.wait_ge(y_stored, (m + 1) * 16)
                sp.sem_inc(halves_out, 1)

            def body(r, first):
                for h in range(2):
                    if h or not first:
                        finish(2 * r + h - 1, 1 - h, PACKS)
                    if not first:
                        store_y(2 * r + h - 2, h, results(r, h))

            def last(m):
                finish(m, 1, SP_PACKS)
                store_y(m - 1, 0, results(ROUNDS, 0))
                store_y(m, 1, results(ROUNDS, 0) + MLP_STEPS)
            rounds(sp, body, last)
            sp.wait_ge(ids_bc_loaded, 16 * (2 * ROUNDS + 1))

        @block.gpsimd
        def _(pool):
            pool.memset(ident[:, :], 0.0).then_inc(ident_zeroed, 1)
            pool.iota(row_id[:, :], pattern=[[1, CHUNKS]], base=0, channel_multiplier=CHUNKS).then_inc(row_id_ready, 1)
            pool.wait_ge(ident_zeroed, 1)
            pool.affine_select(out=ident[:, :], in_=ident[:, :], compare_op=ALU.not_equal, fill=1.0,
                               base=0, pattern=[[-1, P]], channel_multiplier=1).then_inc(ident_ready, 1)
            pool.wait_ge(ids_loaded, 16)

            def body(r, first):
                for t in range(TILES):
                    if not first:
                        pool.wait_ge(ids_ready, (r - 1) * TILES + t + 1)
                        pool.wait_ge(rows_ready, ((r - 1) * TILES + t + 1) * NGR)
                        pool.sem_inc(slots_taken, 1)
                    idx = ids_all if first else ids_now
                    for g, features in enumerate(GROUPS):
                        for f in features:
                            pool.indirect_dma_start(
                                out=emb[:, t, f, :], out_offset=None, in_=gather_tables[f],
                                in_offset=bass.IndirectOffsetOnAxis(ap=idx[:, t, f:f + 1].bitcast(U32), axis=0),
                            ).then_inc(gathered[t][g], 16)

            def last(m):
                pool.wait_ge(mlp_ready, (m - 1) * MLP_STEPS)
                pool.wait_ge(stored, (m + 1) * 16)
                load_packs(pool, grams[m], 1, POOL_PACKS, pool=True)
            rounds(pool, body, last)

        @block.tensor
        def _(pe):
            def bank(before, at, n):
                if not isinstance(before, int) or before + n >= BANKS:
                    pe.wait_ge(copied, before + n - BANKS + 1)
                return work[:, (at + n) % BANKS, :]

            def select(r, h, j):
                out = bank(results(r, h), HALF_BANK[h], j)
                for c in range(CHUNKS):
                    at = j * CHUNKS + c
                    pe.wait_ge(onehot_ready, (2 * r + h) * SEL_PAIRS * CHUNKS + at + 1)
                    for i in range(PAIR):
                        if c == 0:
                            pe.wait_ge(table_lo, PAIR * j + i + 1)
                        cols = slice(i * HALF, (i + 1) * HALF)
                        for part in (tab_hi, tab_lo):
                            mm = nc.tensor.matmul(out[:, cols], part[0:K, PAIR * j + i, c, :],
                                                  onehot[0:K, at % OH_RING, cols],
                                                  start=(c == 0 and i == 0 and part is tab_hi),
                                                  stop=(c == CHUNKS - 1 and part is tab_lo), skip_group_check=True)
                    mm.then_inc(onehot_used, 1)

            def rows(r, h, i):
                t = 2 * h + i
                for g, features in enumerate(GROUPS):
                    pe.wait_ge(gathered[t][g], (r + 1) * 16 * len(features))
                    out = bank(results(r, h), HALF_BANK[h], ROWS_AT[i] + g)
                    for j, f in enumerate(features):
                        last = nc.tensor.transpose(out[:, j * P:(j + 1) * P], emb[:, t, f, :], ident[:, :])
                    last.then_inc(rows_ready, 1)

            def products(r, first, h, i):
                pe.wait_ge(copied, results(r, h) + ROWS_AT[i] + NGR)
                for u in range(SPANS):
                    n = i * SPANS + u
                    if not first or h or n >= 2:
                        pe.wait_ge(extracted_act if n % 2 else extracted_dve, (2 * r + h) * (GRAM_HALF // 2) + n // 2)
                    for j in range(SPAN):
                        a = (u * SPAN + j) * QUADS
                        four = embT[:, i, a:a + QUADS, :]
                        last = nc.tensor.matmul(gram[:, n % 2, j, 0:QUADS * NG], four.rearrange("d s f -> d (s f)"),
                                                four[:, :, 0:NG], start=True, stop=True)
                    last.then_inc(grammed, 1)

            def bottom_rows(turn, par, before, at):
                pe.wait_ge(bot_loaded[par], (turn + 1) * 16)
                out = bank(before, at, 0)
                for b in range(HALF // P):
                    last = nc.tensor.transpose(out[:, b * P:(b + 1) * P], bot[:, par, b, :], ident[:, :])
                last.then_inc(mlp_ready, 1)

            def top(half, before, at):
                pe.wait_ge(w1_split, W1_SPLITS)
                pe.wait_ge(copied, before + 1)
                blocks = [work[:, (at + 1 + m) % BANKS, 0:HALF] for m in range(M1)]
                for n, c in enumerate(X_ORDER):
                    k = X_ROWS[c]
                    if c == CH:
                        pe.wait_ge(bottom_split, half + 1)
                    else:
                        pe.wait_ge(packed_split, half * CH + n)
                    for m, out in enumerate(blocks):
                        cols = slice(m * P, (m + 1) * P)
                        nc.tensor.matmul(out, w1_hi[0:k, c, cols], x_hi[0:k, c, :], start=(n == 0), stop=False)
                        nc.tensor.matmul(out, w1_hi[0:k, c, cols], x_lo[0:k, c, :], start=False, stop=False)
                        last = nc.tensor.matmul(out, w1_lo[0:k, c, cols], x_hi[0:k, c, :], start=False, stop=(n == CH))
                        if n == CH:
                            last.then_inc(mlp_ready, 1)
                for m in range(M2):
                    out = work[:, (at + 1 + M1 + m) % BANKS, 0:HALF]
                    for c in range(M1):
                        if m == 0:
                            pe.wait_ge(copied, before + 2 + c)
                        last = nc.tensor.matmul(out, w2[:, c, m * P:(m + 1) * P], h1[:, c, :], start=(c == 0), stop=(c == M1 - 1))
                    last.then_inc(mlp_ready, 1)
                out = work[:, (at + 1 + M1 + M2) % BANKS, 0:HALF]
                for c in range(M2):
                    pe.wait_ge(copied, before + 2 + M1 + c)
                    last = nc.tensor.matmul(out[0:1, :], w3[:, c:c + 1], h2[:, c, :], start=(c == 0), stop=(c == M2 - 1))
                last.then_inc(mlp_ready, 1)

            pe.wait_ge(ident_ready, 1)

            def body(r, first):
                for h in range(2):
                    for kind, j in FEATURE_STEPS:
                        (select if kind == "select" else rows)(r, h, j)
                    products(r, first, h, 0)
                    if h or not first:
                        bottom_rows(r + h - 1, 1 - h, results(r, h) + FT_HALF, MLP_BANK[h])
                    products(r, first, h, 1)
                    if h or not first:
                        top(2 * r + h - 1, results(r, h) + FT_HALF, MLP_BANK[h])

            def last(m):
                bottom_rows(m // 2, 1, results(ROUNDS, 0), 0)
                top(m, results(ROUNDS, 0), 0)
            rounds(pe, body, last)

        def extract(eng, copy, done, r, first, h, n):
            eng.wait_ge(grammed, (2 * r + h) * GRAM_HALF + n + 1)
            if h or not first:
                eng.wait_ge(stored, (2 * r + h) * 16)
            at = n * SPAN
            for s in range(QUADS):
                own = slice(QS * s, QS * (s + 1))
                last = copy(inter[own, :, at:at + SPAN],
                            gram[own, n % 2, :, s * NG:(s + 1) * NG].rearrange("f j g -> f g j"))
            last.then_inc(done, 1)

        @block.vector
        def _(dve):
            dve.wait_ge(row_id_ready, 1)
            nc.vector.tensor_copy(row_idf[:, :], row_id[:, :]).then_inc(row_idf_ready, 1)
            dve.memset(ids_all[:, ROUNDS * TILES:, :], 0).then_inc(pads_zeroed, 1)
            dve.memset(embT[:, :, :, NF:QS], 0.0).then_inc(pads_zeroed, 1)
            dve.wait_ge(pads_zeroed, 2)
            dve.wait_ge(row_idf_ready, 1)

            def split(i):
                dve.wait_ge(table_hi, i + 1)
                nc.vector.tensor_tensor(tab_lo[0:K, i, :, :].rearrange("p c d -> p (c d)"), stage[i % STAGE][0:K, :],
                                        tab_hi[0:K, i, :, :].rearrange("p c d -> p (c d)").bitcast(F32), ALU.subtract).then_inc(table_lo, 1)

            def onehots(r, first, h, j, chunks):
                dve.wait_ge(ids_bc_loaded, (2 * r + h + 1) * 16)
                for c in chunks:
                    at = j * CHUNKS + c
                    if not first or h or at >= OH_RING:
                        dve.wait_ge(onehot_used, (2 * r + h) * SEL_PAIRS * CHUNKS + at - OH_RING + 1)
                    nc.vector.tensor_scalar(onehot[0:K, at % OH_RING, :],
                                            ids_bc[0:K, PAIR * j:PAIR * (j + 1), :].rearrange("p i n -> p (i n)"),
                                            row_idf[0:K, c:c + 1], None, ALU.is_equal).then_inc(onehot_ready, 1)

            def onehots_of_half(r, h, first):
                for j in range(SEL_PAIRS):
                    if first and h == 0 and j:
                        for i in range(PAIR * j, PAIR * (j + 1)):
                            split(i)
                    onehots(r, first, h, j, range(OH_RING if j == 0 else 0, CHUNKS))

            def split_w1():
                dve.wait_ge(weights_loaded, N_WEIGHTS)
                nc.vector.tensor_tensor(bot_uses[:, 0, :], bot_uses[:, 0, :], bot_uses[:, 1, :], ALU.add).then_inc(w1_bot_summed, 1)
                full = PAIR_ROWS[2]
                parts = [(slice(0, P), slice(0, 2), w1_raw[0]), (slice(0, full), slice(2, 3), w1_raw[1]),
                         (slice(0, P), slice(3, 4), bot_uses[:, 0:1, :])]
                for rows, cs, raw in parts:
                    if raw is parts[2][2]:
                        dve.wait_ge(w1_bot_summed, 1)
                    nc.vector.tensor_copy(w1_hi[rows, cs, :], raw[rows, :, :]).then_inc(w1_hi_ready, 1)
                for n, (rows, cs, raw) in enumerate(parts):
                    dve.wait_ge(w1_hi_ready, n + 1)
                    nc.vector.tensor_tensor(w1_lo[rows, cs, :], raw[rows, :, :], w1_hi[rows, cs, :].bitcast(F32),
                                            ALU.subtract).then_inc(w1_split, 1)

            def split_packed(half, par):
                for n, c in enumerate(X_ORDER[1:]):
                    k = X_ROWS[c]
                    dve.wait_ge(packed_hi_ready, half * CH + n + 1)
                    nc.vector.tensor_tensor(x_lo[0:k, c, :], packed[0:k, par, c, :], x_hi[0:k, c, :].bitcast(F32),
                                            ALU.subtract).then_inc(packed_split, 1)

            def split_bottom(half, before):
                dve.wait_ge(bottom_hi_ready, half + 1)
                dve.wait_ge(copied, before + 1)
                nc.vector.tensor_tensor(x_lo[:, CH, :], botT[:, :], x_hi[:, CH, :].bitcast(F32), ALU.subtract).then_inc(bottom_split, 1)

            for i in range(PAIR):
                split(i)
            onehots(0, True, 0, 0, range(OH_RING))
            dve.wait_ge(ids_loaded, 16)

            def body(r, first):
                for h in range(2):
                    onehots_of_half(r, h, first)
                    if h == 0 and first:
                        split_w1()
                    if h or not first:
                        split_packed(2 * r + h - 1, 1 - h)
                    for t in (2 * h, 2 * h + 1):
                        dve.wait_ge(rows_ready, (r * TILES + t + 1) * NGR)
                        src = ids_all[:, TILES + t, :] if first else ids_all[:, bass.ds((r + 1) * TILES + t, 1), :].rearrange("p o f -> p (o f)")
                        nc.vector.tensor_copy(ids_now[:, t, :], src).then_inc(ids_ready, 1)
                    for n in range(0, GRAM_HALF, 2):
                        extract(dve, nc.vector.tensor_copy, extracted_dve, r, first, h, n)
                        if n == SPANS and (h or not first):
                            split_bottom(2 * r + h - 1, results(r, h) + FT_HALF)
                        if h == 0:
                            onehots(r, first, 1, 0, [n // 2])
                        else:
                            onehots(r + 1, False, 0, 0, [n // 2])

            def last(m):
                split_bottom(m, results(ROUNDS, 0))
                split_packed(m, 1)
            rounds(dve, body, last)

        @block.scalar
        def _(act):
            for i in range(NSEL):
                act.wait_ge(table_staged[i % STAGE], 32 * (i // STAGE + 1))
                nc.scalar.copy(tab_hi[0:K, i, :, :].rearrange("p c d -> p (c d)"), stage[i % STAGE][0:K, :]).then_inc(table_hi, 1)
            for c, k in enumerate(PAIR_ROWS):
                act.dma_start(w1_raw[c // 2][0:k, c % 2, :], w_top1[D + c * P:D + c * P + k, :]).then_inc(weights_loaded, 16)
            act.wait_ge(table_lo, NSEL)
            act.dma_start(bot_uses[:, 0, :], w_top1[0:D, :]).then_inc(weights_loaded, 16)
            act.dma_start(bot_uses[:, 1, :], w_top1[D + PAIRS:, :]).then_inc(weights_loaded, 16)
            act.dma_start(w2[:, :, :], w_top2.rearrange("(c p) n -> p c n", p=P)).then_inc(weights_loaded, 16)
            with nc.allow_non_contiguous_dma(reason="a few hundred elements"):
                act.dma_start(w3[:, :], w_top3.rearrange("(c p) one -> p (c one)", p=P)).then_inc(weights_loaded, 16)
                act.dma_start(b1[:, :], b_top1.rearrange("(c p) -> p c", p=P)).then_inc(weights_loaded, 16)
                act.dma_start(b2[:, :], b_top2.rearrange("(c p) -> p c", p=P)).then_inc(weights_loaded, 16)
            act.wait_ge(pads_zeroed, 2)

            def round_packed(turn, par, pool_packs):
                packs = [pack for pack in PACKS if pack not in pool_packs]
                for c in X_ORDER[1:]:
                    k = X_ROWS[c]
                    of_chunk = [len([x for x in some if x[3] == c]) for some in (PACKS, packs, pool_packs)]
                    act.wait_ge(packs_loaded[par][c], turn * 16 * of_chunk[0] + 16 * of_chunk[1])
                    if of_chunk[2]:
                        act.wait_ge(packs_pool[c], 16 * of_chunk[2])
                    nc.scalar.copy(x_hi[0:k, c, :], packed[0:k, par, c, :]).then_inc(packed_hi_ready, 1)

            def features(r, first, h):
                if not first or h:
                    act.wait_ge(grammed, (2 * r + h) * GRAM_HALF)
                for j in range(SEL_PAIRS):
                    if j == SEL_PAIRS - 1 and (h or not first):
                        round_packed(r + h - 1, 1 - h, [])
                    f = NGA + PAIR * j
                    act.wait_ge(onehot_used, ((2 * r + h) * SEL_PAIRS + j + 1) * CHUNKS)
                    nc.scalar.copy(embT[:, :, :, f:f + PAIR].rearrange("d i b f -> d f (i b)"),
                                   work[:, (HALF_BANK[h] + j) % BANKS, :].rearrange("d (f b) -> d f b", b=HALF)).then_inc(copied, 1)
                act.wait_ge(onehot_ready, (2 * r + h + 1) * SEL_PAIRS * CHUNKS)
                load_ids_bc(act, 2 * r + h + 1)
                for i in range(2):
                    for g, features in enumerate(GROUPS):
                        f, k = features[0], len(features)
                        act.wait_ge(rows_ready, (r * TILES + 2 * h + i) * NGR + g + 1)
                        nc.scalar.copy(embT[:, i, :, f:f + k].rearrange("d b f -> d f b"),
                                       work[:, (HALF_BANK[h] + ROWS_AT[i] + g) % BANKS, 0:k * P].rearrange("d (f b) -> d f b", b=P)).then_inc(copied, 1)

            def bottom_rows(half, at):
                act.wait_ge(mlp_ready, half * MLP_STEPS + 1)
                nc.scalar.copy(x_hi[:, CH, :], work[:, at, 0:HALF]).then_inc(bottom_hi_ready, 1)
                nc.scalar.copy(botT[:, :], work[:, at, 0:HALF]).then_inc(copied, 1)

            def top(half, par, at):
                n = 1
                for h, b, blocks in ((h1, b1, M1), (h2, b2, M2)):
                    for m in range(blocks):
                        act.wait_ge(mlp_ready, half * MLP_STEPS + n + 1)
                        nc.scalar.activation(h[:, m, :], work[:, (at + n) % BANKS, 0:HALF], ACT.Relu, bias=b[:, m:m + 1]).then_inc(copied, 1)
                        n += 1
                act.wait_ge(mlp_ready, half * MLP_STEPS + n + 1)
                nc.scalar.copy(y[:, par, :], work[0:1, (at + n) % BANKS, 0:HALF]).then_inc(copied, 1)

            def body(r, first):
                for h in range(2):
                    features(r, first, h)
                    for n in range(1, GRAM_HALF, 2):
                        if n == SPANS + 1 and (h or not first):
                            bottom_rows(2 * r + h - 1, MLP_BANK[h])
                        extract(act, nc.scalar.copy, extracted_act, r, first, h, n)
                    if h or not first:
                        top(2 * r + h - 1, 1 - h, MLP_BANK[h])

            def last(m):
                bottom_rows(m, 0)
                round_packed(m // 2, 1, POOL_PACKS)
                top(m, 1, 0)
            rounds(act, body, last)


NF = 27
D = 128


def kernel(**inputs):
    import numpy as _np
    import concourse.bacc as _bacc
    from concourse import mybir as _mybir
    from concourse.bass_utils import run_bass_kernel_spmd as _run

    nc = _bacc.Bacc("TRN2", target_bir_lowering=False, num_devices=1)
    arrays = {}

    def take(name, a):
        a = _np.ascontiguousarray(a)
        arrays[f"in_{name}"] = a
        return nc.dram_tensor(f"in_{name}", a.shape, _mybir.dt.from_np(a.dtype), kind="ExternalInput").ap()

    by_rows = sorted(range(NF), key=lambda f: (inputs[f"tbl_{f}"].shape[0], f))
    selected = sorted(by_rows[:SELECTED])
    gathered = sorted(by_rows[SELECTED:])
    order = gathered + selected
    w = _np.asarray(inputs["W_top1"])
    pairs = [(max(order[f], order[g]), min(order[f], order[g])) for f in range(NF) for g in range(f)]
    at = [D + a * (a - 1) // 2 + b for a, b in pairs]
    w = _np.concatenate([w[:D], w[_np.array(at)], w[D + len(at):]])
    ids = _np.asarray(inputs["ids"])
    ids = ids.reshape(-1, QUADS, HALF // P, QS, NF).transpose(0, 2, 3, 1, 4).reshape(ids.shape)
    sel_ids = ids[:, selected].reshape(-1, HALF, SELECTED).transpose(0, 2, 1)
    sel_ids = _np.concatenate([sel_ids, _np.zeros_like(sel_ids[:1])])[:, None]

    args = [take("bottom", inputs["r_bottom_mlp_out"]), take("ids", ids[:, gathered]), take("sel_ids", sel_ids),
            [take(f"tbl_{f}", inputs[f"tbl_{f}"]) for f in gathered],
            [take(f"tbl_{f}", inputs[f"tbl_{f}"]) for f in selected], take("W_top1", w)]
    args += [take(n, inputs[n]) for n in ("b_top1", "W_top2", "b_top2", "W_top3")]
    out = nc.dram_tensor("out_0", (ids.shape[0], 1), F32, kind="ExternalOutput").ap()
    dlrm_tower(nc, *args, out)
    r = _run(nc, [arrays], core_ids=[0])
    return r.results[0]["out_0"]
```
